# Optimizing a Trainium2 kernel written in Bass

```python
import numpy as np
import jax
import jax.numpy as jnp

def _softmax(x, axis=-1):
    return jax.nn.softmax(x, axis=axis)

def _gelu(x):
    return jax.nn.gelu(x, approximate=True)

def _silu(x):
    return jax.nn.silu(x)

def _sigmoid(x):
    return jax.nn.sigmoid(x)

def _layernorm(x, axis=-1, eps=1e-05):
    m = jnp.mean(x, axis=axis, keepdims=True)
    v = jnp.var(x, axis=axis, keepdims=True)
    return (x - m) / jnp.sqrt(v + eps)

def _scatter_add(tgt, idx, src, axis=0):
    return tgt.at[idx].add(src)

def _segment_sum(src, seg, n):
    return jax.ops.segment_sum(src, seg, n)
kernel_name = 'mk_dlrm_tower_d1_rec_r8_90fccf'

def setup_inputs(seed: int=0):
    np.random.seed(seed)
    _w = jnp.asarray

    def _rec_inputs():
        import jax
        import jax.numpy as jnp
        _tk = jax.random.key(seed)
        ids = jnp.stack([jax.random.randint(jax.random.fold_in(_tk, 200 + f), (512,), 0, v, jnp.int32) for f, v in enumerate([1250, 1000, 1250, 1250, 12500, 1250, 125000, 1000, 12500, 1250, 1250, 1250, 12500, 1000, 12500, 12500, 1000, 12500, 1250, 1000, 1250, 1000, 12500, 1000, 1250, 1000])], axis=1)
        tbl_0 = 0.05 * jax.random.normal(jax.random.fold_in(_tk, 500 + 0), (1250, 128), jnp.float32)
        tbl_1 = 0.05 * jax.random.normal(jax.random.fold_in(_tk, 500 + 1), (1000, 128), jnp.float32)
        tbl_2 = 0.05 * jax.random.normal(jax.random.fold_in(_tk, 500 + 2), (1250, 128), jnp.float32)
        tbl_3 = 0.05 * jax.random.normal(jax.random.fold_in(_tk, 500 + 3), (1250, 128), jnp.float32)
        tbl_4 = 0.05 * jax.random.normal(jax.random.fold_in(_tk, 500 + 4), (12500, 128), jnp.float32)
        tbl_5 = 0.05 * jax.random.normal(jax.random.fold_in(_tk, 500 + 5), (1250, 128), jnp.float32)
        tbl_6 = 0.05 * jax.random.normal(jax.random.fold_in(_tk, 500 + 6), (125000, 128), jnp.float32)
        tbl_7 = 0.05 * jax.random.normal(jax.random.fold_in(_tk, 500 + 7), (1000, 128), jnp.float32)
        tbl_8 = 0.05 * jax.random.normal(jax.random.fold_in(_tk, 500 + 8), (12500, 128), jnp.float32)
        tbl_9 = 0.05 * jax.random.normal(jax.random.fold_in(_tk, 500 + 9), (1250, 128), jnp.float32)
        tbl_10 = 0.05 * jax.random.normal(jax.random.fold_in(_tk, 500 + 10), (1250, 128), jnp.float32)
        tbl_11 = 0.05 * jax.random.normal(jax.random.fold_in(_tk, 500 + 11), (1250, 128), jnp.float32)
        tbl_12 = 0.05 * jax.random.normal(jax.random.fold_in(_tk, 500 + 12), (12500, 128), jnp.float32)
        tbl_13 = 0.05 * jax.random.normal(jax.random.fold_in(_tk, 500 + 13), (1000, 128), jnp.float32)
        tbl_14 = 0.05 * jax.random.normal(jax.random.fold_in(_tk, 500 + 14), (12500, 128), jnp.float32)
        tbl_15 = 0.05 * jax.random.normal(jax.random.fold_in(_tk, 500 + 15), (12500, 128), jnp.float32)
        tbl_16 = 0.05 * jax.random.normal(jax.random.fold_in(_tk, 500 + 16), (1000, 128), jnp.float32)
        tbl_17 = 0.05 * jax.random.normal(jax.random.fold_in(_tk, 500 + 17), (12500, 128), jnp.float32)
        tbl_18 = 0.05 * jax.random.normal(jax.random.fold_in(_tk, 500 + 18), (1250, 128), jnp.float32)
        tbl_19 = 0.05 * jax.random.normal(jax.random.fold_in(_tk, 500 + 19), (1000, 128), jnp.float32)
        tbl_20 = 0.05 * jax.random.normal(jax.random.fold_in(_tk, 500 + 20), (1250, 128), jnp.float32)
        tbl_21 = 0.05 * jax.random.normal(jax.random.fold_in(_tk, 500 + 21), (1000, 128), jnp.float32)
        tbl_22 = 0.05 * jax.random.normal(jax.random.fold_in(_tk, 500 + 22), (12500, 128), jnp.float32)
        tbl_23 = 0.05 * jax.random.normal(jax.random.fold_in(_tk, 500 + 23), (1000, 128), jnp.float32)
        tbl_24 = 0.05 * jax.random.normal(jax.random.fold_in(_tk, 500 + 24), (1250, 128), jnp.float32)
        tbl_25 = 0.05 * jax.random.normal(jax.random.fold_in(_tk, 500 + 25), (1000, 128), jnp.float32)
        _rk = jax.random.fold_in(_tk, 7)
        r_dense_features = -0.000520686 + 1.00062 * jax.random.normal(jax.random.fold_in(_rk, 101), (512, 128), jnp.float32)
        W_top1 = 0.0405887 * jax.random.normal(jax.random.fold_in(_tk, 801), (607, 512), jnp.float32)
        W_top2 = 0.0441942 * jax.random.normal(jax.random.fold_in(_tk, 802), (512, 256), jnp.float32)
        W_top3 = 0.0625 * jax.random.normal(jax.random.fold_in(_tk, 803), (256, 1), jnp.float32)
        b_top1 = jnp.zeros((512,), jnp.float32)
        b_top2 = jnp.zeros((256,), jnp.float32)
        return (r_dense_features, ids, tbl_0, tbl_1, tbl_2, tbl_3, tbl_4, tbl_5, tbl_6, tbl_7, tbl_8, tbl_9, tbl_10, tbl_11, tbl_12, tbl_13, tbl_14, tbl_15, tbl_16, tbl_17, tbl_18, tbl_19, tbl_20, tbl_21, tbl_22, tbl_23, tbl_24, tbl_25, W_top1, b_top1, W_top2, b_top2, W_top3)
    r_dense_features, ids, tbl_0, tbl_1, tbl_2, tbl_3, tbl_4, tbl_5, tbl_6, tbl_7, tbl_8, tbl_9, tbl_10, tbl_11, tbl_12, tbl_13, tbl_14, tbl_15, tbl_16, tbl_17, tbl_18, tbl_19, tbl_20, tbl_21, tbl_22, tbl_23, tbl_24, tbl_25, W_top1, b_top1, W_top2, b_top2, W_top3 = _rec_inputs()

    def _L0_rec_setup():
        import jax, jax.numpy as jnp
        import numpy as np
        NUM_SPARSE = 26
        EMBED_DIM = 128
        BATCH = 2048
        key = jax.random.key(seed)
        k1, k2 = jax.random.split(key)
        dense_features = jax.random.normal(k1, (BATCH, EMBED_DIM), dtype=jnp.float32)
        sparse_features = jax.random.normal(k2, (BATCH, NUM_SPARSE, EMBED_DIM), dtype=jnp.float32)
        return {'dense_features': dense_features, 'sparse_features': sparse_features}
    _L0_rec_all = _L0_rec_setup()
    _L0_rec_in = {k: v for k, v in _L0_rec_all.items() if k in ()}
    del _L0_rec_all
    return {'r_dense_features': r_dense_features, 'ids': ids, 'tbl_0': tbl_0, 'tbl_1': tbl_1, 'tbl_2': tbl_2, 'tbl_3': tbl_3, 'tbl_4': tbl_4, 'tbl_5': tbl_5, 'tbl_6': tbl_6, 'tbl_7': tbl_7, 'tbl_8': tbl_8, 'tbl_9': tbl_9, 'tbl_10': tbl_10, 'tbl_11': tbl_11, 'tbl_12': tbl_12, 'tbl_13': tbl_13, 'tbl_14': tbl_14, 'tbl_15': tbl_15, 'tbl_16': tbl_16, 'tbl_17': tbl_17, 'tbl_18': tbl_18, 'tbl_19': tbl_19, 'tbl_20': tbl_20, 'tbl_21': tbl_21, 'tbl_22': tbl_22, 'tbl_23': tbl_23, 'tbl_24': tbl_24, 'tbl_25': tbl_25, 'W_top1': W_top1, 'b_top1': b_top1, 'W_top2': W_top2, 'b_top2': b_top2, 'W_top3': W_top3}

def reference(r_dense_features, ids, tbl_0, tbl_1, tbl_2, tbl_3, tbl_4, tbl_5, tbl_6, tbl_7, tbl_8, tbl_9, tbl_10, tbl_11, tbl_12, tbl_13, tbl_14, tbl_15, tbl_16, tbl_17, tbl_18, tbl_19, tbl_20, tbl_21, tbl_22, tbl_23, tbl_24, tbl_25, W_top1, b_top1, W_top2, b_top2, W_top3):
    import jax
    import jax.numpy as jnp

    def _L0_rec_ref(dense_features, sparse_features):
        import jax, jax.numpy as jnp
        import numpy as np
        NUM_SPARSE = 26
        EMBED_DIM = 128
        BATCH = 2048
        F = NUM_SPARSE + 1
        combined = jnp.concatenate([dense_features[:, None, :], sparse_features], axis=1)
        interactions = jnp.einsum('bfd,bgd->bfg', combined, combined)
        iu, ju = jnp.triu_indices(F, k=1)
        interactions_flat = interactions[:, iu, ju]
        return jnp.concatenate([dense_features, interactions_flat], axis=1)
    e = jnp.stack([tbl_0[ids[:, 0]], tbl_1[ids[:, 1]], tbl_2[ids[:, 2]], tbl_3[ids[:, 3]], tbl_4[ids[:, 4]], tbl_5[ids[:, 5]], tbl_6[ids[:, 6]], tbl_7[ids[:, 7]], tbl_8[ids[:, 8]], tbl_9[ids[:, 9]], tbl_10[ids[:, 10]], tbl_11[ids[:, 11]], tbl_12[ids[:, 12]], tbl_13[ids[:, 13]], tbl_14[ids[:, 14]], tbl_15[ids[:, 15]], tbl_16[ids[:, 16]], tbl_17[ids[:, 17]], tbl_18[ids[:, 18]], tbl_19[ids[:, 19]], tbl_20[ids[:, 20]], tbl_21[ids[:, 21]], tbl_22[ids[:, 22]], tbl_23[ids[:, 23]], tbl_24[ids[:, 24]], tbl_25[ids[:, 25]]], axis=1)
    z = _L0_rec_ref(r_dense_features, e)
    z = z.reshape(z.shape[0], -1)
    h = jnp.concatenate([z, r_dense_features], axis=1)
    h = jnp.maximum(h @ W_top1 + b_top1, 0.0)
    h = jnp.maximum(h @ W_top2 + b_top2, 0.0)
    y = h @ W_top3
    return y

_drawn_inputs = setup_inputs


def setup_inputs(seed=0):
    import zlib

    import numpy as np

    out = dict(_drawn_inputs(seed))
    spreads = {'b_top1': (0.0, 0.1), 'b_top2': (0.0, 0.1)}
    factors = {}
    for name, (base, spread) in spreads.items():
        noise = np.random.default_rng([zlib.crc32(name.encode()), seed]).standard_normal(out[name].shape)
        drawn = base * np.exp(spread * noise) if base else spread * noise
        out[name] = jnp.asarray(drawn.astype(out[name].dtype))
    for name, factor in factors.items():
        out[name] = (out[name] * factor).astype(out[name].dtype)
    return out
```

```python
from contextlib import ExitStack

import concourse.bass as bass
from concourse import mybir

F32 = mybir.dt.float32
F32R = mybir.dt.float32r
I32 = mybir.dt.int32
ALU = mybir.AluOpType
ACT = mybir.ActivationFunctionType

TABLES = 26
FEATURES = TABLES + 1
SLOTS = 32
ONE_HOT_TABLES = (18, 20, 22, 24)
ONE_HOT_TABLES = (19, 21, 23, 25)
GROUPS = ((25, 23, 21, 19), (18, 17, 16, 15), (14, 13, 12, 11), (10, 9, 8, 7), (6, 5, 4, 3), (2, 1))


def dlrm_program(nc, ids, one_hot_ids, dense, tables, w1, w2, columns, y):
    batch, dim = dense.shape
    P = 128
    tiles = batch // P
    hidden1, hidden2 = w1.shape[1], w2.shape[1]
    n1, n2 = hidden1 // P, hidden2 // P
    n_pairs = FEATURES * (FEATURES - 1) // 2
    pair_parts = -(-(FEATURES - 1) // 4)
    quads_half = 8
    halves = P // 4 // quads_half
    n_hot = len(ONE_HOT_TABLES)
    hot_rows = [next(r for r in range(128, 0, -1) if tables[i].shape[0] % r == 0) for i in ONE_HOT_TABLES]
    hot_parts = [tables[i].shape[0] // r for i, r in zip(ONE_HOT_TABLES, hot_rows)]
    max_parts = max(hot_parts)
    gathered = [f for g in GROUPS for f in g]
    assert sorted(gathered + [i + 1 for i in ONE_HOT_TABLES] + [0]) == list(range(FEATURES))

    with ExitStack() as ctx:
        def sbuf(name, shape, dt=F32):
            return ctx.enter_context(nc.sbuf_tensor(name, shape, dt))

        def psum(name, shape):
            return ctx.enter_context(nc.psum_tensor(name, shape, F32))

        def sem(name):
            return ctx.enter_context(nc.semaphore(name))

        ids_all = sbuf("ids_all", [P, tiles, TABLES], I32)
        rows = sbuf("rows", [P, len(gathered), dim])
        dense_rows = sbuf("dense_rows", [P, tiles, dim])
        whole_t = sbuf("whole_t", [P, 1 + n_hot, batch])
        features_t = sbuf("features_t", [P, P, SLOTS])
        pairs = sbuf("pairs", [P, pair_parts, P])
        w_pairs = sbuf("w_pairs", [P, pair_parts, hidden1])
        w_dense = sbuf("w_dense", [P, 2, hidden1])
        w_dense_sum = sbuf("w_dense_sum", [P, hidden1])
        w2_sb = sbuf("w2_sb", [P, n1, hidden2])
        columns_sb = sbuf("columns_sb", [P, n1 + n2 + n2])
        b1_sb, b2_sb, w3_sb = columns_sb[:, 0:n1], columns_sb[:, n1:n1 + n2], columns_sb[:, n1 + n2:n1 + 2 * n2]
        hidden1_t = sbuf("hidden1_t", [P, n1, P])
        hidden2_t = sbuf("hidden2_t", [P, n2, P])
        y_row = sbuf("y_row", [1, batch])
        ident = sbuf("ident", [P, P])
        row_ids = sbuf("row_ids", [P, n_hot, max_parts])
        hot_ids = sbuf("hot_ids", [P, n_hot, batch], I32)
        table_sb = sbuf("table_sb", [P, n_hot, max_parts * dim])
        table_hi = sbuf("table_hi", [P, 2, max_parts * dim], F32R)
        table_lo = sbuf("table_lo", [P, 2, max_parts * dim], F32R)
        one_hot = sbuf("one_hot", [P, 4, batch], F32R)

        turn_ps = psum("turn_ps", [P, 2, 512])
        gram_ps = psum("gram_ps", [P, 2, quads_half, P])
        layer_ps = psum("layer_ps", [P, 2, 512])

        ids_in, dense_in, hot_ids_in = sem("ids_in"), sem("dense_in"), sem("hot_ids_in")
        table_in = [sem(f"table_in{n}") for n in range(n_hot)]
        w_zeroed, weights_in = sem("w_zeroed"), sem("weights_in")
        w_dense_summed = sem("w_dense_summed")
        ident_zeroed, ident_made, row_ids_made = sem("ident_zeroed"), sem("ident_made"), sem("row_ids_made")
        pads_zeroed = sem("pads_zeroed")
        hi_made, lo_made, one_hot_made = sem("hi_made"), sem("lo_made"), sem("one_hot_made")
        one_hot_used, whole_made = sem("one_hot_used"), sem("whole_made")
        dense_turned = sem("dense_turned")
        gathered_in = [sem(f"gathered_in{n}") for n in range(len(GROUPS))]
        turned = [sem(f"turned{n}") for n in range(len(GROUPS))]
        turned_out_act, turned_out_dve = sem("turned_out_act"), sem("turned_out_dve")
        whole_placed = sem("whole_placed")
        gram_done, pairs_act, pairs_dve = sem("gram_done"), sem("pairs_act"), sem("pairs_dve")
        layer1_done, layer1_out = sem("layer1_done"), sem("layer1_out")
        layer2_done, layer2_out = sem("layer2_done"), sem("layer2_out")
        layer3_done, y_out, y_stored = sem("layer3_done"), sem("y_out"), sem("y_stored")

        n_groups = len(GROUPS)
        act_groups = [g for g in range(n_groups) if g % 2 == 0]
        dve_groups = [g for g in range(n_groups) if g % 2 == 1]
        first_of = [sum(len(g) for g in GROUPS[:n]) for n in range(n_groups)]
        slots = features_t[:, :, :].rearrange("p b s -> p s b")

        def turned_out(engine, t, n):
            if n % 2 == 0:
                engine.wait_ge(turned_out_act, t * len(act_groups) + n // 2 + 1)
            else:
                engine.wait_ge(turned_out_dve, t * len(dve_groups) + n // 2 + 1)

        def group_slots(n):
            g = GROUPS[n]
            step = g[1] - g[0]
            assert all(b - a == step for a, b in zip(g, g[1:]))
            stop = g[-1] + step
            return slice(g[0], stop if stop >= 0 else None, step)

        def copy_turned(copy, n, bank):
            g = GROUPS[n]
            lo, step = g[-1], g[0] - g[1]
            src = turn_ps[:, bank, 0:len(g) * P].rearrange("p (s b) -> p s b", b=P)
            return copy(slots[:, lo:g[0] + 1:step, :], src)

        def copy_pairs(copy, j, half):
            ring = half % 2
            for k in range(4):
                count = len(range(k, FEATURES - 1, 4))
                src = gram_ps[32 * j:32 * j + 32, ring, :, FEATURES * j + k:FEATURES * j + k + 4 * (count - 1) + 1:4]
                first = half * quads_half * 4 + j
                dst = pairs[32 * k:32 * k + 32, 0:count, first:first + 4 * (quads_half - 1) + 1:4]
                last = copy(dst, src.rearrange("p q i -> p i q"))
            return last

        with nc.Block() as block:

            @block.sync
            def _(sp):
                sp.dma_start(ids_all[:, :, :], ids.rearrange("(t p) f -> p t f", p=P)).then_inc(ids_in, 16)
                hot_src = one_hot_ids.rearrange("(o n) b -> o n b", o=1).broadcast_to([P, n_hot, batch])
                sp.dma_start(hot_ids[:, :, :], hot_src).then_inc(hot_ids_in, 16)
                for n, i in enumerate(ONE_HOT_TABLES):
                    sp.dma_start(table_sb[0:hot_rows[n], n, 0:hot_parts[n] * dim],
                                 tables[i].rearrange("(p c) d -> p (c d)", c=hot_parts[n])).then_inc(table_in[n], 16)
                sp.dma_start(w_dense[:, 0, :], w1[0:dim, :]).then_inc(weights_in, 16)
                sp.dma_start(w_dense[:, 1, :], w1[dim + n_pairs:2 * dim + n_pairs, :]).then_inc(weights_in, 16)
                sp.wait_ge(w_zeroed, 1)
                row = dim
                for left in range(FEATURES - 1):
                    count = FEATURES - 1 - left
                    first = 32 * (left % 4) + left + 1
                    sp.dma_start(w_pairs[first:first + count, left // 4, :], w1[row:row + count, :]).then_inc(weights_in, 16)
                    row += count
                sp.dma_start(w2_sb[:, :, :], w2.rearrange("(c p) n -> p c n", p=P)).then_inc(weights_in, 16)
                with sp.Fori(0, tiles) as t:
                    sp.wait_ge(y_out, t + 1)
                    sp.dma_start(y.rearrange("(o b) c -> o (b c)", o=1)[:, bass.ds(t * P, P)],
                                 y_row[0:1, bass.ds(t * P, P)]).then_inc(y_stored, 16)
                sp.wait_ge(y_stored, 16 * tiles)

            @block.gpsimd
            def _(pool):
                nc.gpsimd.memset(ident[:, :], 0.0).then_inc(ident_zeroed, 1)
                for n in range(n_hot):
                    nc.gpsimd.iota(row_ids[:, n, 0:hot_parts[n]], pattern=[[1, hot_parts[n]]], base=0,
                                   channel_multiplier=hot_parts[n], allow_small_or_imprecise_dtypes=True).then_inc(row_ids_made, 1)
                pool.wait_ge(ident_zeroed, 1)
                nc.gpsimd.affine_select(out=ident[:, :], in_=ident[:, :], compare_op=ALU.not_equal, fill=1.0,
                                        base=0, pattern=[[-1, P]], channel_multiplier=1).then_inc(ident_made, 1)
                pool.wait_ge(ids_in, 16)
                for t in range(tiles):
                    for n, group in enumerate(GROUPS):
                        if t >= 1:
                            pool.wait_ge(turned[n], t)
                        for m, f in enumerate(group):
                            pool.indirect_dma_start(rows[:, first_of[n] + m, :], None, tables[f - 1],
                                                    bass.IndirectOffsetOnAxis(ap=ids_all[:, t, f - 1:f], axis=0)).then_inc(gathered_in[n], 16)

            @block.scalar
            def _(act):
                act.dma_start(dense_rows[:, :, :], dense.rearrange("(t p) d -> p t d", p=P)).then_inc(dense_in, 16)
                act.dma_start(columns_sb[:, :], columns).then_inc(weights_in, 16)
                for n in range(n_hot):
                    act.wait_ge(table_in[n], 16)
                    if n >= 2:
                        act.wait_ge(one_hot_used, sum(hot_parts[:n - 1]))
                    r, c = hot_rows[n], hot_parts[n] * dim
                    nc.scalar.activation(table_hi[0:r, n % 2, 0:c], table_sb[0:r, n, 0:c], ACT.Copy).then_inc(hi_made, 1)
                    if n == 0:
                        act.wait_ge(dense_turned, 1)
                        nc.scalar.activation(whole_t[:, 0, :], turn_ps[:, 1, :], ACT.Copy).then_inc(whole_made, 1)
                    if n >= 1:
                        act.wait_ge(one_hot_used, sum(hot_parts[:n]))
                        nc.scalar.activation(whole_t[:, n, :], turn_ps[:, (n - 1) % 2, :], ACT.Copy).then_inc(whole_made, 1)
                act.wait_ge(one_hot_used, sum(hot_parts[:n_hot]))
                nc.scalar.activation(whole_t[:, n_hot, :], turn_ps[:, (n_hot - 1) % 2, :], ACT.Copy).then_inc(whole_made, 1)
                act.wait_ge(weights_in, 16 * n_weight_loads)
                def tile(t, first):
                    if not first:
                        act.wait_ge(layer1_done, t)
                    for n in act_groups:
                        act.wait_ge(turned[n], t + 1)
                        copy_turned(act.copy, n, n % 2).then_inc(turned_out_act, 1)
                    for half in range(halves):
                        act.wait_ge(gram_done, t * halves + half + 1)
                        for j in (0, 1):
                            last = copy_pairs(act.copy, j, half)
                        last.then_inc(pairs_act, 1)
                    act.wait_ge(layer1_done, t + 1)
                    for m in range(n1):
                        nc.scalar.activation(hidden1_t[:, m, :], layer_ps[:, 0, m * P:(m + 1) * P], ACT.Relu,
                                             bias=b1_sb[:, m:m + 1]).then_inc(layer1_out, 1)
                    act.wait_ge(layer2_done, t + 1)
                    for m in range(n2):
                        nc.scalar.activation(hidden2_t[:, m, :], layer_ps[:, 1, m * P:(m + 1) * P], ACT.Relu,
                                             bias=b2_sb[:, m:m + 1]).then_inc(layer2_out, 1)
                    act.wait_ge(layer3_done, t + 1)
                    nc.scalar.activation(y_row[0:1, bass.ds(t * P, P)], layer_ps[0:1, 1, n2 * P:(n2 + 1) * P], ACT.Copy).then_inc(y_out, 1)

                tile(0, first=True)
                with act.Fori(1, tiles) as t:
                    tile(t, first=False)

            @block.vector
            def _(dve):
                nc.vector.memset(w_pairs[:, :, :], 0.0).then_inc(w_zeroed, 1)
                dve.wait_ge(row_ids_made, n_hot)
                dve.wait_ge(hot_ids_in, 16)
                made = 0
                for n in range(n_hot):
                    r, c = hot_rows[n], hot_parts[n] * dim
                    dve.wait_ge(hi_made, n + 1)
                    nc.vector.tensor_tensor(table_lo[0:r, n % 2, 0:c], table_sb[0:r, n, 0:c],
                                            table_hi[0:r, n % 2, 0:c].bitcast(F32), ALU.subtract).then_inc(lo_made, 1)
                    for c in range(hot_parts[n]):
                        if made >= 4:
                            dve.wait_ge(one_hot_used, made - 3)
                        nc.vector.tensor_scalar(one_hot[0:r, made % 4, :], hot_ids[0:r, n, :], row_ids[0:r, n, c:c + 1],
                                                None, ALU.is_equal).then_inc(one_hot_made, 1)
                        made += 1
                nc.vector.memset(features_t[:, :, FEATURES:SLOTS], 0.0).then_inc(pads_zeroed, 1)
                nc.vector.memset(pairs[:, pair_parts - 1, :], 0.0).then_inc(pads_zeroed, 1)
                dve.wait_ge(pads_zeroed, 2)
                dve.wait_ge(weights_in, 16 * n_weight_loads)
                nc.vector.tensor_tensor(w_dense_sum[:, :], w_dense[:, 0, :], w_dense[:, 1, :], ALU.add).then_inc(w_dense_summed, 1)
                dve.wait_ge(whole_made, 1 + n_hot)
                def tile(t, first):
                    if not first:
                        dve.wait_ge(layer1_done, t)
                    hot = [i + 1 for i in ONE_HOT_TABLES]
                    nc.vector.tensor_copy(slots[:, hot[0]:hot[-1] + 1:2, :], whole_t[:, 1:1 + n_hot, bass.ds(t * P, P)])
                    nc.vector.tensor_copy(slots[:, 0, :], whole_t[:, 0, bass.ds(t * P, P)]).then_inc(whole_placed, 1)
                    for n in dve_groups:
                        dve.wait_ge(turned[n], t + 1)
                        copy_turned(nc.vector.tensor_copy, n, n % 2).then_inc(turned_out_dve, 1)
                    for half in range(halves):
                        dve.wait_ge(gram_done, t * halves + half + 1)
                        for j in (2, 3):
                            last = copy_pairs(nc.vector.tensor_copy, j, half)
                        last.then_inc(pairs_dve, 1)

                tile(0, first=True)
                with dve.Fori(1, tiles) as t:
                    tile(t, first=False)

            @block.tensor
            def _(pe):
                pe.wait_ge(ident_made, 1)
                pe.wait_ge(dense_in, 16)
                for t in range(tiles):
                    last = nc.tensor.transpose(turn_ps[:, 1, t * P:(t + 1) * P], dense_rows[:, t, :], ident[:, :])
                last.then_inc(dense_turned, 1)
                made = 0
                for n in range(n_hot):
                    pe.wait_ge(lo_made, n + 1)
                    if n >= 1:
                        pe.wait_ge(whole_made, n)
                    r = hot_rows[n]
                    for c in range(hot_parts[n]):
                        pe.wait_ge(one_hot_made, made + 1)
                        nc.tensor.matmul(turn_ps[:, n % 2, :], table_hi[0:r, n % 2, c * dim:(c + 1) * dim],
                                         one_hot[0:r, made % 4, :], start=(c == 0), stop=False)
                        last = nc.tensor.matmul(turn_ps[:, n % 2, :], table_lo[0:r, n % 2, c * dim:(c + 1) * dim],
                                                one_hot[0:r, made % 4, :], start=False, stop=(c == hot_parts[n] - 1))
                        made += 1
                        last.then_inc(one_hot_used, 1)
                pe.wait_ge(whole_made, 1 + n_hot)
                pe.wait_ge(w_dense_summed, 1)
                def tile(t, first):
                    for n, group in enumerate(GROUPS):
                        pe.wait_ge(gathered_in[n], (t + 1) * 16 * len(group))
                        if n >= 2:
                            turned_out(pe, t, n - 2)
                        for m in range(len(group)):
                            at = len(group) - 1 - m
                            last = nc.tensor.transpose(turn_ps[:, n % 2, at * P:(at + 1) * P], rows[:, first_of[n] + m, :], ident[:, :])
                        last.then_inc(turned[n], 1)
                    turned_out(pe, t, n_groups - 2)
                    turned_out(pe, t, n_groups - 1)
                    pe.wait_ge(whole_placed, t + 1)
                    for half in range(halves):
                        if half >= 2:
                            pe.wait_ge(pairs_act, t * halves + half - 1)
                            pe.wait_ge(pairs_dve, t * halves + half - 1)
                        for q in range(quads_half):
                            s = (half * quads_half + q) * 4
                            last = nc.tensor.matmul(gram_ps[:, half % 2, q, 0:4 * FEATURES],
                                                    features_t[:, s:s + 4, :],
                                                    features_t[:, s:s + 4, 0:FEATURES], start=True, stop=True)
                        last.then_inc(gram_done, 1)
                    pe.wait_ge(pairs_act, (t + 1) * halves)
                    pe.wait_ge(pairs_dve, (t + 1) * halves)
                    for m in range(n1):
                        out = layer_ps[:, 0, m * P:(m + 1) * P]
                        nc.tensor.matmul(out, w_dense_sum[:, m * P:(m + 1) * P], features_t[:, :, 0], start=True, stop=False)
                        for i in range(pair_parts):
                            last = nc.tensor.matmul(out, w_pairs[:, i, m * P:(m + 1) * P], pairs[:, i, :],
                                                    start=False, stop=(i == pair_parts - 1))
                    last.then_inc(layer1_done, 1)
                    if not first:
                        pe.wait_ge(y_out, t)
                    for m in range(n2):
                        for i in range(n1):
                            if m == 0:
                                pe.wait_ge(layer1_out, t * n1 + i + 1)
                            last = nc.tensor.matmul(layer_ps[:, 1, m * P:(m + 1) * P], w2_sb[:, i, m * P:(m + 1) * P],
                                                    hidden1_t[:, i, :], start=(i == 0), stop=(i == n1 - 1))
                    last.then_inc(layer2_done, 1)
                    pe.wait_ge(layer2_out, (t + 1) * n2)
                    for i in range(n2):
                        last = nc.tensor.matmul(layer_ps[0:1, 1, n2 * P:(n2 + 1) * P], w3_sb[:, i:i + 1],
                                                hidden2_t[:, i, :], start=(i == 0), stop=(i == n2 - 1))
                    last.then_inc(layer3_done, 1)

                tile(0, first=True)
                with pe.Fori(1, tiles) as t:
                    tile(t, first=False)


n_weight_loads = 2 + (FEATURES - 1) + 1 + 1


def kernel(**inputs):
    import numpy as _np
    import concourse.bacc as _bacc
    from concourse import mybir as _mybir
    from concourse.bass_utils import run_bass_kernel_spmd as _run

    nc = _bacc.Bacc("TRN2", target_bir_lowering=False, num_devices=1)
    arrays, aps = {}, {}

    def give(name, a):
        a = _np.ascontiguousarray(a)
        arrays[f"in_{name}"] = a
        aps[name] = nc.dram_tensor(f"in_{name}", a.shape, _mybir.dt.from_np(a.dtype), kind="ExternalInput").ap()

    give("ids", inputs["ids"])
    give("one_hot_ids", _np.asarray(inputs["ids"]).T[list(ONE_HOT_TABLES)])
    for name in ("r_dense_features", "W_top1", "W_top2"):
        give(name, inputs[name])
    give("columns", _np.concatenate([_np.asarray(inputs[name]).reshape(-1, 128).T for name in ("b_top1", "b_top2", "W_top3")], axis=1))
    for i in range(TABLES):
        give(f"tbl_{i}", inputs[f"tbl_{i}"])
    y = nc.dram_tensor("y", (aps["ids"].shape[0], 1), _mybir.dt.float32, kind="ExternalOutput").ap()
    dlrm_program(nc, aps["ids"], aps["one_hot_ids"], aps["r_dense_features"], [aps[f"tbl_{i}"] for i in range(TABLES)],
                 aps["W_top1"], aps["W_top2"], aps["columns"], y)
    r = _run(nc, [arrays], core_ids=[0])
    return r.results[0]["y"]
```

```python
from contextlib import ExitStack

import numpy as np

import concourse.bass as bass
from concourse import mybir

F32 = mybir.dt.float32
F32R = mybir.dt.float32r
I32 = mybir.dt.int32
ALU = mybir.AluOpType
ACT = mybir.ActivationFunctionType

TABLES = 26
FEATURES = TABLES + 1
SLOTS = 32
COLUMNS = 14
PAIR_PARTS = 4
HOT = (1, 7, 13, 16, 19, 21)
GATHERED = tuple(i for i in range(TABLES) if i not in HOT)
GATHERS = len(GATHERED) // 2
GROUPS = tuple(range(min(4, GATHERS - n)) for n in range(0, GATHERS, 4))
EARLY = (2, 4)
FEATURE_OF = (0, *(1 + i for i in HOT), *(1 + i for i in GATHERED))


def pair_places():
    for k in range(4):
        for g in range(SLOTS):
            for i in range(PAIR_PARTS):
                c = 4 * i + k
                if g >= FEATURES or c >= COLUMNS:
                    yield 32 * k + g, i, None, False
                elif c + 1 <= g <= c + 13:
                    yield 32 * k + g, i, (c, g), False
                elif c + 14 < FEATURES and g != c + 14:
                    yield 32 * k + g, i, (min(g, c + 14), max(g, c + 14)), True
                else:
                    yield 32 * k + g, i, None, False


def dlrm_program(nc, ids, table_starts, gathered_tables, hot_ids, hot_tables, dense, w_dense, w_pairs, w2, columns,
                 late_rows, y):
    batch, dim = dense.shape
    P = 128
    tiles, units, unit = batch // P, 2, 64
    hidden1, hidden2 = w_pairs.shape[2], w2.shape[1]
    n1, n2 = hidden1 // P, hidden2 // P
    quads = 8
    halves = unit // 4 // quads
    n_hot = len(HOT)
    hot_rows = [next(r for r in range(P, 0, -1) if table.shape[0] % r == 0) for table in hot_tables]
    hot_parts = [table.shape[0] // r for table, r in zip(hot_tables, hot_rows)]
    max_parts = max(hot_parts)
    n_groups = len(GROUPS)
    ring = 6
    hot_list = [(n, c) for n in range(n_hot) for c in range(hot_parts[n])]
    act_share = [i for i, (n, c) in enumerate(hot_list) if c % 4 == 3]
    assert halves == 2 and n_groups == 3 and hidden1 == 512 and 1 + n_hot + 2 * GATHERS == FEATURES

    with ExitStack() as ctx:
        def sbuf(name, shape, dt=F32):
            return ctx.enter_context(nc.sbuf_tensor(name, shape, dt))

        def psum(name, shape):
            return ctx.enter_context(nc.psum_tensor(name, shape, F32))

        def sem(name):
            return ctx.enter_context(nc.semaphore(name))

        ids_sb = sbuf("ids_sb", [P, tiles * units, GATHERS], I32)
        starts_sb = sbuf("starts_sb", [P, GATHERS], I32)
        row_at = sbuf("row_at", [P, tiles * units, GATHERS], I32)
        rows = sbuf("rows", [P, tiles * units, GATHERS, dim])
        dense_rows = sbuf("dense_rows", [P, tiles, dim])
        whole_t = sbuf("whole_t", [P, 1 + n_hot, batch])
        features_t = sbuf("features_t", [P, P, SLOTS])
        pairs = sbuf("pairs", [P, PAIR_PARTS, P])
        late_sb = sbuf("late_sb", [P, PAIR_PARTS], I32)
        w_pairs_sb = sbuf("w_pairs_sb", [P, PAIR_PARTS, hidden1])
        w_dense_sb = sbuf("w_dense_sb", [P, 2, hidden1])
        w_dense_sum = sbuf("w_dense_sum", [P, hidden1])
        w2_sb = sbuf("w2_sb", [P, n1, hidden2])
        columns_sb = sbuf("columns_sb", [P, n1 + n2 + n2])
        b1_sb, b2_sb, w3_sb = columns_sb[:, 0:n1], columns_sb[:, n1:n1 + n2], columns_sb[:, n1 + n2:n1 + 2 * n2]
        hidden1_t = sbuf("hidden1_t", [P, n1, P])
        hidden2_t = sbuf("hidden2_t", [P, n2, P])
        y_row = sbuf("y_row", [1, batch])
        ident = sbuf("ident", [P, P])
        row_ids = sbuf("row_ids", [P, n_hot, max_parts])
        hot_ids_sb = sbuf("hot_ids_sb", [P, n_hot, batch], I32)
        table_sb = sbuf("table_sb", [P, n_hot, max_parts * dim])
        table_hi = sbuf("table_hi", [P, 3, max_parts * dim], F32R)
        table_lo = sbuf("table_lo", [P, 3, max_parts * dim], F32R)
        distance = sbuf("distance", [P, batch])
        one_hot = sbuf("one_hot", [P, ring, batch], F32R)

        turn_ps = psum("turn_ps", [P, 3, 512])
        gram_ps = psum("gram_ps", [P, 2, quads, P])
        dense_ps = psum("dense_ps", [P, 512])

        ids_in, dense_in, rows_found = sem("ids_in"), sem("dense_in"), sem("rows_found")
        hot_in = [sem(f"hot_in{n}") for n in range(n_hot)]
        weights_in = sem("weights_in")
        w_dense_summed, start_zeroed = sem("w_dense_summed"), sem("start_zeroed")
        ident_zeroed, ident_made, row_ids_made = sem("ident_zeroed"), sem("ident_made"), sem("row_ids_made")
        hi_made, lo_made, distance_made = sem("hi_made"), sem("lo_made"), sem("distance_made")
        one_hot_dve, one_hot_act = sem("one_hot_dve"), sem("one_hot_act")
        one_hot_used, whole_made, dense_turned = sem("one_hot_used"), sem("whole_made"), sem("dense_turned")
        rows_in = [[sem(f"rows_in{at}_{n}") for n in range(n_groups)] for at in range(tiles * units)]
        turned = [[sem(f"turned{u}{n}") for n in range(n_groups)] for u in range(units)]
        placed_act, placed_dve, whole_placed = sem("placed_act"), sem("placed_dve"), sem("whole_placed")
        gram_done, pairs_plain, pairs_whole = sem("gram_done"), sem("pairs_plain"), sem("pairs_whole")
        layer1_done, layer1_out = sem("layer1_done"), sem("layer1_out")
        layer2_done, layer2_out = sem("layer2_done"), sem("layer2_out")
        layer3_done, y_out, y_stored = sem("layer3_done"), sem("y_out"), sem("y_stored")

        n_weight_loads = 5
        act_groups, dve_groups = range(0, n_groups, 2), range(1, n_groups, 2)
        slots = features_t[:, :, :].rearrange("p b s -> p s b")

        def wait_placed(engine, t, u, n):
            if n in act_groups:
                engine.wait_ge(placed_act, (t * units + u) * len(act_groups) + n // 2 + 1)
            else:
                engine.wait_ge(placed_dve, (t * units + u) * len(dve_groups) + n // 2 + 1)

        def place(copy, u, n):
            slot = 1 + n_hot + 8 * n
            count = 2 * len(GROUPS[n])
            src = turn_ps[:, n, 0:count * unit].rearrange("p (s b) -> p s b", b=unit)
            return copy(slots[:, slot:slot + count, u * unit:(u + 1) * unit], src)

        def pair_block(u, half, j, k, first, count):
            at = FEATURES * j + first + k
            src = gram_ps[32 * j:32 * j + 32, half, :, at:at + 4 * (count - 1) + 1:4].rearrange("p q i -> p i q")
            b = u * unit + half * quads * 4 + j
            return pairs[32 * k:32 * k + 32, 0:count, b:b + 4 * (quads - 1) + 1:4], src

        def hot_bank(n):
            return gram_ps[:, n % 2, 0:4, :].rearrange("p q c -> p (q c)")

        layer1_at = [dense_ps[:, m * P:(m + 1) * P] for m in range(n1)]
        layer2_at = [dense_ps[:, m * P:(m + 1) * P] for m in range(n2)]
        layer3_at = dense_ps[0:1, n2 * P:(n2 + 1) * P]
        last_layer1_at = [layer1_at[0], layer1_at[1], turn_ps[:, 0, 0:P], turn_ps[:, 0, P:2 * P]]
        last_layer2_at = [turn_ps[:, 1 + m, 0:P] for m in range(n2)]
        last_layer3_at = gram_ps[0:1, 0, 0, :]

        y_line = y.rearrange("(o b) c -> o (b c)", o=1)

        with nc.Block() as block:

            @block.sync
            def _(sp):
                sp.dma_start(ids_sb[:, :, :], ids).then_inc(ids_in, 16)
                sp.dma_start(starts_sb[:, :], table_starts).then_inc(ids_in, 16)
                for n, table in enumerate(hot_tables):
                    sp.dma_start(hot_ids_sb[:, n, :], hot_ids[n:n + 1, :].broadcast_to([P, batch])).then_inc(hot_in[n], 16)
                    if n > 0:
                        sp.dma_start(table_sb[0:hot_rows[n], n, 0:hot_parts[n] * dim],
                                     table.rearrange("(p c) d -> p (c d)", c=hot_parts[n])).then_inc(hot_in[n], 16)
                sp.dma_start(late_sb[:, :], late_rows).then_inc(weights_in, 16)
                sp.dma_start(w_dense_sb[:, :, :], w_dense.rearrange("c p n -> p c n")).then_inc(weights_in, 16)
                sp.dma_start(w_pairs_sb[:, :, :], w_pairs).then_inc(weights_in, 16)
                sp.dma_start(w2_sb[:, :, :], w2.rearrange("(c p) n -> p c n", p=P)).then_inc(weights_in, 16)
                with sp.Fori(0, tiles) as t:
                    sp.wait_ge(y_out, t + 1)
                    sp.dma_start(y_line[:, bass.ds(t * P, P)], y_row[0:1, bass.ds(t * P, P)]).then_inc(y_stored, 16)
                sp.wait_ge(y_stored, 16 * tiles)

            @block.gpsimd
            def _(pool):
                nc.gpsimd.memset(ident[:, :], 0.0).then_inc(ident_zeroed, 1)
                for n in range(n_hot):
                    nc.gpsimd.iota(row_ids[:, n, 0:hot_parts[n]], pattern=[[1, hot_parts[n]]], base=0,
                                   channel_multiplier=hot_parts[n], allow_small_or_imprecise_dtypes=True).then_inc(row_ids_made, 1)
                pool.wait_ge(ident_zeroed, 1)
                nc.gpsimd.affine_select(out=ident[:, :], in_=ident[:, :], compare_op=ALU.not_equal, fill=1.0,
                                        base=0, pattern=[[-1, P]], channel_multiplier=1).then_inc(ident_made, 1)
                pool.wait_ge(rows_found, 1)
                for t in range(tiles):
                    for u in range(units):
                        for n, group in enumerate(GROUPS):
                            for m in group:
                                at = t * units + u
                                pool.indirect_dma_start(rows[:, at, 4 * n + m, :], None, gathered_tables,
                                                        bass.IndirectOffsetOnAxis(ap=row_at[:, at, 4 * n + m:4 * n + m + 1], axis=0)
                                                        ).then_inc(rows_in[at][n], 16)

            @block.scalar
            def _(act):
                act.dma_start(table_sb[0:hot_rows[0], 0, 0:hot_parts[0] * dim],
                              hot_tables[0].rearrange("(p c) d -> p (c d)", c=hot_parts[0])).then_inc(hot_in[0], 16)
                act.dma_start(dense_rows[:, :, :], dense.rearrange("(t p) d -> p t d", p=P)).then_inc(dense_in, 16)
                act.dma_start(columns_sb[:, :], columns).then_inc(weights_in, 16)

                def place_groups(t, u):
                    if t >= 1:
                        act.wait_ge(gram_done, ((t - 1) * units + u + 1) * halves)
                    for n in act_groups:
                        act.wait_ge(turned[u][n], t + 1)
                        place(act.copy, u, n).then_inc(placed_act, 1)

                def one_hot_part(i):
                    n, c = hot_list[i]
                    r = hot_rows[n]
                    if i >= ring:
                        act.wait_ge(one_hot_used, i - ring + 1)
                    if act_share.index(i) >= 1:
                        act.wait_ge(one_hot_act, act_share.index(i))
                    nc.scalar.activation(distance[0:r, :], hot_ids_sb[0:r, n, :], ACT.Abs, scale=-1.0,
                                         bias=row_ids[0:r, n, c:c + 1]).then_inc(distance_made, 1)
                    act.wait_ge(distance_made, act_share.index(i) + 1)
                    nc.scalar.activation(one_hot[0:r, i % ring, :], distance[0:r, :], ACT.Relu, scale=-1.0,
                                         bias=1.0).then_inc(one_hot_act, 1)

                def high_part(n):
                    act.wait_ge(hot_in[n], 32)
                    if n >= 3:
                        act.wait_ge(one_hot_used, sum(hot_parts[:n - 2]))
                    r, c = hot_rows[n], hot_parts[n] * dim
                    nc.scalar.activation(table_hi[0:r, n % 3, 0:c], table_sb[0:r, n, 0:c], ACT.Copy).then_inc(hi_made, 1)

                def copy_whole(n):
                    act.wait_ge(one_hot_used, sum(hot_parts[:n + 1]))
                    nc.scalar.activation(whole_t[:, n + 1, :], hot_bank(n), ACT.Copy).then_inc(whole_made, 1)

                high_part(0)
                act.wait_ge(dense_turned, 1)
                nc.scalar.activation(whole_t[:, 0, :], turn_ps[:, 0, :], ACT.Copy).then_inc(whole_made, 1)
                high_part(1)
                act.wait_ge(row_ids_made, n_hot)
                for n in range(n_hot):
                    share = [i for i in act_share if hot_list[i][0] == n]
                    one_hot_part(share[0])
                    if n >= 1:
                        copy_whole(n - 1)
                    if n + 2 < n_hot:
                        high_part(n + 2)
                    for i in share[1:]:
                        one_hot_part(i)
                    if n - 1 in EARLY:
                        act.wait_ge(start_zeroed, 2)
                        place_groups(0, EARLY.index(n - 1))
                copy_whole(n_hot - 1)
                act.wait_ge(weights_in, 16 * n_weight_loads)

                def plain_pairs(t, u):
                    for half in range(halves):
                        act.wait_ge(gram_done, (t * units + u) * halves + half + 1)
                        for j in range(4):
                            for k in range(4):
                                last = act.copy(*pair_block(u, half, j, k, 0, len(range(k, COLUMNS, 4))))
                            last.then_inc(pairs_plain, 1)

                def layer1_relu(t, at, one_bank):
                    for m in range(n1):
                        if one_bank and m == 0:
                            act.wait_ge(layer1_done, 2 * t + 2)
                        if not one_bank and m % 2 == 0:
                            act.wait_ge(layer1_done, 2 * t + m // 2 + 1)
                        nc.scalar.activation(hidden1_t[:, m, :], at[m], ACT.Relu, bias=b1_sb[:, m:m + 1]).then_inc(layer1_out, 1)

                def layer2_relu(t, at):
                    act.wait_ge(layer2_done, t + 1)
                    for m in range(n2):
                        nc.scalar.activation(hidden2_t[:, m, :], at[m], ACT.Relu, bias=b2_sb[:, m:m + 1]).then_inc(layer2_out, 1)

                def results(t, at, own):
                    act.wait_ge(layer3_done, t + 1)
                    nc.scalar.activation(y_row[0:1, own], at, ACT.Copy).then_inc(y_out, 1)

                for t in range(tiles):
                    last = t == tiles - 1
                    plain_pairs(t, 0)
                    if t >= 1:
                        if last:
                            layer2_relu(t - 1, layer2_at)
                        place_groups(t, 1)
                        if not last:
                            layer2_relu(t - 1, layer2_at)
                    plain_pairs(t, 1)
                    if not last:
                        place_groups(t + 1, 0)
                    if t >= 1:
                        results(t - 1, layer3_at, slice((t - 1) * P, t * P))
                    layer1_relu(t, last_layer1_at if last else layer1_at, one_bank=not last)
                layer2_relu(tiles - 1, last_layer2_at)
                results(tiles - 1, last_layer3_at, slice(batch - P, batch))

            @block.vector
            def _(dve):
                nc.vector.memset(features_t[:, :, FEATURES:SLOTS], 0.0).then_inc(start_zeroed, 1)
                nc.vector.memset(pairs[:, PAIR_PARTS - 1, :], 0.0).then_inc(start_zeroed, 1)
                dve.wait_ge(ids_in, 32)
                starts = starts_sb[:, :].rearrange("p (o g) -> p o g", o=1).broadcast_to([P, tiles * units, GATHERS])
                nc.vector.tensor_tensor(row_at[:, :, :], ids_sb[:, :, :], starts, ALU.add).then_inc(rows_found, 1)
                dve.wait_ge(row_ids_made, n_hot)

                def place_whole(t, u):
                    b = t * P + u * unit
                    nc.vector.tensor_copy(slots[:, 0:1 + n_hot, u * unit:(u + 1) * unit],
                                          whole_t[:, :, b:b + unit]).then_inc(whole_placed, 1)

                def place_groups(t, u):
                    if t >= 1:
                        dve.wait_ge(gram_done, ((t - 1) * units + u + 1) * halves)
                        place_whole(t, u)
                    for n in dve_groups:
                        dve.wait_ge(turned[u][n], t + 1)
                        place(nc.vector.tensor_copy, u, n).then_inc(placed_dve, 1)

                def low_part(n):
                    r, c = hot_rows[n], hot_parts[n] * dim
                    dve.wait_ge(hi_made, n + 1)
                    nc.vector.tensor_tensor(table_lo[0:r, n % 3, 0:c], table_sb[0:r, n, 0:c],
                                            table_hi[0:r, n % 3, 0:c].bitcast(F32), ALU.subtract).then_inc(lo_made, 1)

                low_part(0)
                for i, (n, c) in enumerate(hot_list):
                    r = hot_rows[n]
                    if c == 0:
                        dve.wait_ge(hot_in[n], 32)
                    if i not in act_share:
                        if i >= ring:
                            dve.wait_ge(one_hot_used, i - ring + 1)
                        nc.vector.tensor_scalar(one_hot[0:r, i % ring, :], hot_ids_sb[0:r, n, :], row_ids[0:r, n, c:c + 1],
                                                None, ALU.is_equal).then_inc(one_hot_dve, 1)
                    if c == 1 and n + 1 < n_hot:
                        low_part(n + 1)
                    if c == 4 and n - 1 in EARLY:
                        dve.wait_ge(start_zeroed, 2)
                        place_groups(0, EARLY.index(n - 1))
                dve.wait_ge(weights_in, 16 * n_weight_loads)
                nc.vector.tensor_tensor(w_dense_sum[:, :], w_dense_sb[:, 0, :], w_dense_sb[:, 1, :], ALU.add).then_inc(w_dense_summed, 1)
                dve.wait_ge(whole_made, 1 + n_hot)

                def late_pairs(t, u):
                    for half in range(halves):
                        for j in range(4):
                            dve.wait_ge(pairs_plain, ((t * units + u) * halves + half) * 4 + j + 1)
                            for k in range(4):
                                count = len(range(k, FEATURES - COLUMNS, 4))
                                dst, src = pair_block(u, half, j, k, COLUMNS, count)
                                late = late_sb[32 * k:32 * k + 32, 0:count].rearrange("p (i o) -> p i o", o=1)
                                last = nc.vector.copy_predicated(dst, late.broadcast_to([32, count, quads]), src)
                        last.then_inc(pairs_whole, 1)

                place_whole(0, 0)
                place_whole(0, 1)
                for t in range(tiles):
                    late_pairs(t, 0)
                    if t >= 1:
                        place_groups(t, 1)
                    late_pairs(t, 1)
                    if t + 1 < tiles:
                        place_groups(t + 1, 0)

            @block.tensor
            def _(pe):
                def transpose_groups(t, u):
                    for n, group in enumerate(GROUPS):
                        pe.wait_ge(rows_in[t * units + u][n], 16 * len(group))
                        for m in group:
                            last = nc.tensor.transpose(turn_ps[:, n, m * P:(m + 1) * P], rows[:, t * units + u, 4 * n + m, :], ident[:, :])
                        last.then_inc(turned[u][n], 1)

                def products(t, u, first=False):
                    pe.wait_ge(whole_placed, t * units + u + 1)
                    for n in range(n_groups):
                        wait_placed(pe, t, u, n)
                    for half in range(halves):
                        if not first:
                            pe.wait_ge(pairs_whole, (t * units + u - 1) * halves + half + 1)
                        for q in range(quads):
                            b = u * unit + (half * quads + q) * 4
                            last = nc.tensor.matmul(gram_ps[:, half, q, 0:4 * FEATURES], features_t[:, b:b + 4, :],
                                                    features_t[:, b:b + 4, 0:FEATURES], start=True, stop=True)
                        last.then_inc(gram_done, 1)

                def layer1(t, at):
                    pe.wait_ge(pairs_whole, (t + 1) * units * halves)
                    for m in range(n1):
                        nc.tensor.matmul(at[m], w_dense_sum[:, m * P:(m + 1) * P], whole_t[:, 0, t * P:(t + 1) * P], start=True, stop=False)
                        for i in range(PAIR_PARTS):
                            last = nc.tensor.matmul(at[m], w_pairs_sb[:, i, m * P:(m + 1) * P], pairs[:, i, :],
                                                    start=False, stop=(i == PAIR_PARTS - 1))
                        if m % 2 == 1:
                            last.then_inc(layer1_done, 1)

                def layer2(t):
                    pe.wait_ge(layer1_out, (t + 1) * n1)
                    for m in range(n2):
                        for i in range(n1):
                            last = nc.tensor.matmul(layer2_at[m], w2_sb[:, i, m * P:(m + 1) * P],
                                                    hidden1_t[:, i, :], start=(i == 0), stop=(i == n1 - 1))
                    last.then_inc(layer2_done, 1)

                def layer3(t, at):
                    pe.wait_ge(layer2_out, (t + 1) * n2)
                    for i in range(n2):
                        last = nc.tensor.matmul(at, w3_sb[:, i:i + 1], hidden2_t[:, i, :], start=(i == 0), stop=(i == n2 - 1))
                    last.then_inc(layer3_done, 1)

                pe.wait_ge(ident_made, 1)
                pe.wait_ge(dense_in, 16)
                for t in range(tiles):
                    last = nc.tensor.transpose(turn_ps[:, 0, t * P:(t + 1) * P], dense_rows[:, t, :], ident[:, :])
                last.then_inc(dense_turned, 1)
                for i, (n, c) in enumerate(hot_list):
                    r = hot_rows[n]
                    if c == 0:
                        pe.wait_ge(lo_made, n + 1)
                        if n >= 2:
                            pe.wait_ge(whole_made, n)
                    if i in act_share:
                        pe.wait_ge(one_hot_act, act_share.index(i) + 1)
                    else:
                        pe.wait_ge(one_hot_dve, i + 1 - len([a for a in act_share if a < i]))
                    nc.tensor.matmul(hot_bank(n), table_hi[0:r, n % 3, c * dim:(c + 1) * dim],
                                     one_hot[0:r, i % ring, :], start=(c == 0), stop=False)
                    nc.tensor.matmul(hot_bank(n), table_lo[0:r, n % 3, c * dim:(c + 1) * dim],
                                     one_hot[0:r, i % ring, :], start=False, stop=(c == hot_parts[n] - 1)).then_inc(one_hot_used, 1)
                    if c == hot_parts[n] - 1 and n in EARLY:
                        u = EARLY.index(n)
                        pe.wait_ge(whole_made, 1)
                        if u == 1:
                            for g in range(n_groups):
                                wait_placed(pe, 0, 0, g)
                        transpose_groups(0, u)
                pe.wait_ge(whole_made, 1 + n_hot)
                pe.wait_ge(w_dense_summed, 1)

                for t in range(tiles):
                    last = t == tiles - 1
                    products(t, 0, first=(t == 0))
                    if t >= 1:
                        if last:
                            layer2(t - 1)
                        transpose_groups(t, 1)
                        if not last:
                            layer2(t - 1)
                    products(t, 1)
                    if not last:
                        transpose_groups(t + 1, 0)
                    if t >= 1:
                        layer3(t - 1, layer3_at)
                        pe.wait_ge(y_out, t)
                    layer1(t, last_layer1_at if last else layer1_at)
                for i in range(n1):
                    pe.wait_ge(layer1_out, (tiles - 1) * n1 + i + 1)
                    for m in range(n2):
                        last = nc.tensor.matmul(last_layer2_at[m], w2_sb[:, i, m * P:(m + 1) * P],
                                                hidden1_t[:, i, :], start=(i == 0), stop=(i == n1 - 1))
                last.then_inc(layer2_done, 1)
                layer3(tiles - 1, last_layer3_at)


def kernel(**inputs):
    import numpy as _np
    import concourse.bacc as _bacc
    from concourse import mybir as _mybir
    from concourse.bass_utils import run_bass_kernel_spmd as _run

    nc = _bacc.Bacc("TRN2", target_bir_lowering=False, num_devices=1)
    arrays = {}

    def give(name, a):
        a = _np.ascontiguousarray(a)
        arrays[f"in_{name}"] = a
        return nc.dram_tensor(f"in_{name}", a.shape, _mybir.dt.from_np(a.dtype), kind="ExternalInput").ap()

    w1 = _np.asarray(inputs["W_top1"])
    dim = inputs["r_dense_features"].shape[1]
    pair_row = {}
    for a in range(FEATURES):
        for b in range(a + 1, FEATURES):
            pair_row[a, b] = dim + len(pair_row)
    w_pairs = _np.zeros((128, PAIR_PARTS, w1.shape[1]), w1.dtype)
    late_rows = _np.zeros((128, PAIR_PARTS), _np.int32)
    for p, i, pair, late in pair_places():
        if pair is not None:
            w_pairs[p, i] = w1[pair_row[tuple(sorted(FEATURE_OF[s] for s in pair))]]
            late_rows[p, i] = late
    w_dense = _np.stack([w1[:dim], w1[dim + len(pair_row):]])
    columns = _np.concatenate([_np.asarray(inputs[n]).reshape(-1, 128).T for n in ("b_top1", "b_top2", "W_top3")], axis=1)

    tables = [_np.asarray(inputs[f"tbl_{i}"]) for i in range(TABLES)]
    ids = _np.asarray(inputs["ids"])
    gather_ids = ids[:, list(GATHERED)].reshape(-1, 64, GATHERS, 2).transpose(3, 1, 0, 2).reshape(128, -1, GATHERS)
    starts = _np.cumsum([0] + [tables[i].shape[0] for i in GATHERED])[:-1].astype(_np.int32)
    table_starts = _np.repeat(starts.reshape(GATHERS, 2).T, 64, axis=0)

    args = [
        give("ids", gather_ids),
        give("table_starts", table_starts),
        give("gathered_tables", _np.concatenate([tables[i] for i in GATHERED])),
        give("hot_ids", ids.T[list(HOT)]),
        [give(f"tbl_{i}", tables[i]) for i in HOT],
        give("dense", inputs["r_dense_features"]),
        give("w_dense", w_dense),
        give("w_pairs", w_pairs),
        give("w2", inputs["W_top2"]),
        give("columns", columns),
        give("late_rows", late_rows),
    ]
    y = nc.dram_tensor("y", (inputs["ids"].shape[0], 1), _mybir.dt.float32, kind="ExternalOutput").ap()
    dlrm_program(nc, *args, y)
    r = _run(nc, [arrays], core_ids=[0])
    return r.results[0]["y"]
```

```python
from contextlib import ExitStack

import numpy as np

import concourse.bass as bass
from concourse import mybir

F32 = mybir.dt.float32
F32R = mybir.dt.float32r
I32 = mybir.dt.int32
ALU = mybir.AluOpType
ACT = mybir.ActivationFunctionType

TABLES = 26
FEATURES = TABLES + 1
SLOTS = 32
COLUMNS = 14
PAIR_PARTS = 4
HOT = (1, 7, 13, 16, 19, 21)
GATHERED = tuple(i for i in range(TABLES) if i not in HOT)
GATHERS = len(GATHERED) // 2
GROUPS = tuple(range(min(4, GATHERS - n)) for n in range(0, GATHERS, 4))
EARLY = (2, 4)
FEATURE_OF = (0, *(1 + i for i in HOT), *(1 + i for i in GATHERED))


def pair_places():
    for k in range(4):
        for g in range(SLOTS):
            for i in range(PAIR_PARTS):
                c = 4 * i + k
                if g >= FEATURES or c >= COLUMNS:
                    yield 32 * k + g, i, None, False
                elif c + 1 <= g <= c + 13:
                    yield 32 * k + g, i, (c, g), False
                elif c + 14 < FEATURES and g != c + 14:
                    yield 32 * k + g, i, (min(g, c + 14), max(g, c + 14)), True
                else:
                    yield 32 * k + g, i, None, False


def dlrm_program(nc, ids, gathered_tables, hot_ids, hot_tables, dense, w_dense, w_pairs, w2, columns,
                 late_rows, y):
    batch, dim = dense.shape
    P = 128
    tiles, units, unit = batch // P, 2, 64
    hidden1, hidden2 = w_pairs.shape[2], w2.shape[1]
    n1, n2 = hidden1 // P, hidden2 // P
    quads = 8
    halves = unit // 4 // quads
    n_hot = len(HOT)
    hot_rows = [next(r for r in range(P, 0, -1) if table.shape[0] % r == 0) for table in hot_tables]
    hot_parts = [table.shape[0] // r for table, r in zip(hot_tables, hot_rows)]
    max_parts = max(hot_parts)
    n_groups = len(GROUPS)
    ring = 8
    hot_list = [(n, c) for n in range(n_hot) for c in range(hot_parts[n])]
    act_share = [i for i, (n, c) in enumerate(hot_list) if c % 4 == 3]
    assert halves == 2 and n_groups == 3 and hidden1 == 512 and 1 + n_hot + 2 * GATHERS == FEATURES

    with ExitStack() as ctx:
        def sbuf(name, shape, dt=F32):
            return ctx.enter_context(nc.sbuf_tensor(name, shape, dt))

        def psum(name, shape):
            return ctx.enter_context(nc.psum_tensor(name, shape, F32))

        def sem(name):
            return ctx.enter_context(nc.semaphore(name))

        ids_sb = sbuf("ids_sb", [P, tiles * units + 1, GATHERS], I32)
        row_at = sbuf("row_at", [P, tiles * units, GATHERS], I32)
        rows = sbuf("rows", [P, tiles * units, GATHERS, dim])
        dense_rows = sbuf("dense_rows", [P, tiles, dim])
        whole_t = sbuf("whole_t", [P, 1 + n_hot, batch])
        features_t = sbuf("features_t", [P, P, SLOTS])
        pairs = sbuf("pairs", [P, 2, PAIR_PARTS, P])
        late_sb = sbuf("late_sb", [P, PAIR_PARTS], I32)
        w_pairs_sb = sbuf("w_pairs_sb", [P, PAIR_PARTS, hidden1])
        w_dense_sb = sbuf("w_dense_sb", [P, 2, hidden1])
        w_dense_sum = sbuf("w_dense_sum", [P, hidden1])
        w2_sb = sbuf("w2_sb", [P, n1, hidden2])
        columns_sb = sbuf("columns_sb", [P, n1 + n2 + n2])
        b1_sb, b2_sb, w3_sb = columns_sb[:, 0:n1], columns_sb[:, n1:n1 + n2], columns_sb[:, n1 + n2:n1 + 2 * n2]
        hidden1_t = sbuf("hidden1_t", [P, n1, P])
        hidden2_t = sbuf("hidden2_t", [P, 2, n2, P])
        y_row = sbuf("y_row", [1, batch])
        ident = sbuf("ident", [P, P])
        row_ids = sbuf("row_ids", [P, n_hot, max_parts])
        hot_ids_sb = sbuf("hot_ids_sb", [P, n_hot, batch], I32)
        table_sb = sbuf("table_sb", [P, n_hot, max_parts * dim])
        table_hi = sbuf("table_hi", [P, 3, max_parts * dim], F32R)
        table_lo = sbuf("table_lo", [P, 3, max_parts * dim], F32R)
        distance = sbuf("distance", [P, 2, batch])
        one_hot = sbuf("one_hot", [P, ring, batch], F32R)

        turn_ps = psum("turn_ps", [P, 3, 512])
        gram_ps = psum("gram_ps", [P, 2, quads, P])
        dense_ps = psum("dense_ps", [P, 512])

        ids_in, dense_in, rows_found = sem("ids_in"), sem("dense_in"), sem("rows_found")
        hot_in = [sem(f"hot_in{n}") for n in range(n_hot)]
        weights_in = sem("weights_in")
        w_dense_summed, start_zeroed = sem("w_dense_summed"), sem("start_zeroed")
        ident_zeroed, ident_made, row_ids_made = sem("ident_zeroed"), sem("ident_made"), sem("row_ids_made")
        hi_made, lo_made, distance_made = sem("hi_made"), sem("lo_made"), sem("distance_made")
        one_hot_dve, one_hot_act = sem("one_hot_dve"), sem("one_hot_act")
        one_hot_used, whole_made, dense_turned = sem("one_hot_used"), sem("whole_made"), sem("dense_turned")
        rows_in = [[sem(f"rows_in{at}_{n}") for n in range(n_groups)] for at in range(tiles * units)]
        turned = [[sem(f"turned{u}{n}") for n in range(n_groups)] for u in range(units)]
        placed_act, placed_dve, whole_placed = sem("placed_act"), sem("placed_dve"), sem("whole_placed")
        last_placed = sem("last_placed")
        gram_done, pairs_plain, pairs_whole = sem("gram_done"), sem("pairs_plain"), sem("pairs_whole")
        layer1_done, layer1_out = sem("layer1_done"), sem("layer1_out")
        layer2_done, layer2_out, layer2_out_dve = sem("layer2_done"), sem("layer2_out"), sem("layer2_out_dve")
        layer3_done, y_out, y_stored = sem("layer3_done"), sem("y_out"), sem("y_stored")

        n_weight_loads = 5
        act_groups, dve_groups = range(0, n_groups, 2), range(1, n_groups, 2)
        slots = features_t[:, :, :].rearrange("p b s -> p s b")
        flat_features = features_t[:, :, :].rearrange("p b s -> p (b s)")
        quad_rows = 3 * SLOTS + FEATURES

        def wait_placed(engine, t, u, n):
            if n in act_groups:
                engine.wait_ge(placed_act, (t * units + u) * len(act_groups) + n // 2 + 1)
            else:
                engine.wait_ge(placed_dve, (t * units + u) * len(dve_groups) + n // 2 + 1)

        def split_columns(n):
            c = hot_parts[n] * dim
            return [slice(0, c // 2), slice(c // 2, c)] if n == 0 else [slice(0, c)]

        def pieces_made(n):
            return sum(len(split_columns(before)) for before in range(n))

        def place(copy, u, n):
            slot = 1 + n_hot + 8 * n
            count = 2 * len(GROUPS[n])
            src = turn_ps[:, n, 0:count * unit].rearrange("p (s b) -> p s b", b=unit)
            return copy(slots[:, slot:slot + count, u * unit:(u + 1) * unit], src)

        def pair_block(t, u, half, j, k, first, count):
            at = FEATURES * j + first + k
            src = gram_ps[32 * j:32 * j + FEATURES, half, :, at:at + 4 * (count - 1) + 1:4].rearrange("p q i -> p i q")
            b = u * unit + half * quads * 4 + j
            return pairs[32 * k:32 * k + FEATURES, t % 2, 0:count, b:b + 4 * (quads - 1) + 1:4], src

        def hot_bank(n):
            return gram_ps[:, n % 2, 0:4, :].rearrange("p q c -> p (q c)")

        layer1_at = [dense_ps[:, m * P:(m + 1) * P] for m in range(n1)]
        layer2_at = [dense_ps[:, m * P:(m + 1) * P] for m in range(n2)]
        layer3_at = dense_ps[0:1, n2 * P:(n2 + 1) * P]
        last_layer1_at = [*(turn_ps[:, g, 0:P] for g in range(n_groups)), gram_ps[:, 0, 0, :]]
        last_layer2_at = [gram_ps[:, 0, 4, :], gram_ps[:, 1, 0, :]]
        last_layer3_at = gram_ps[0:1, 1, 4, :]

        y_line = y.rearrange("(o b) c -> o (b c)", o=1)

        with nc.Block() as block:

            @block.sync
            def _(sp):
                sp.dma_start(ids_sb[:, :, :], ids).then_inc(ids_in, 16)
                for n, table in enumerate(hot_tables):
                    sp.dma_start(hot_ids_sb[:, n, :], hot_ids[n:n + 1, :].broadcast_to([P, batch])).then_inc(hot_in[n], 16)
                    if n > 0:
                        sp.dma_start(table_sb[0:hot_rows[n], n, 0:hot_parts[n] * dim],
                                     table.rearrange("(p c) d -> p (c d)", c=hot_parts[n])).then_inc(hot_in[n], 16)
                sp.dma_start(late_sb[:, :], late_rows).then_inc(weights_in, 16)
                sp.dma_start(w_dense_sb[:, :, :], w_dense.rearrange("c p n -> p c n")).then_inc(weights_in, 16)
                sp.dma_start(w_pairs_sb[:, :, :], w_pairs).then_inc(weights_in, 16)
                sp.dma_start(w2_sb[:, :, :], w2.rearrange("(c p) n -> p c n", p=P)).then_inc(weights_in, 16)
                with sp.Fori(0, tiles - 2) as t:
                    sp.wait_ge(y_out, t + 1)
                    sp.dma_start(y_line[:, bass.ds(t * P, P)], y_row[0:1, bass.ds(t * P, P)]).then_inc(y_stored, 16)
                sp.wait_ge(y_out, tiles)
                sp.dma_start(y_line[:, (tiles - 2) * P:], y_row[0:1, (tiles - 2) * P:]).then_inc(y_stored, 16)
                sp.wait_ge(y_stored, 16 * (tiles - 1))

            @block.gpsimd
            def _(pool):
                nc.gpsimd.memset(ident[:, :], 0.0).then_inc(ident_zeroed, 1)
                for n in range(n_hot):
                    nc.gpsimd.iota(row_ids[:, n, 0:hot_parts[n]], pattern=[[1, hot_parts[n]]], base=0,
                                   channel_multiplier=hot_parts[n], allow_small_or_imprecise_dtypes=True).then_inc(row_ids_made, 1)
                pool.wait_ge(ident_zeroed, 1)
                nc.gpsimd.affine_select(out=ident[:, :], in_=ident[:, :], compare_op=ALU.not_equal, fill=1.0,
                                        base=0, pattern=[[-1, P]], channel_multiplier=1).then_inc(ident_made, 1)
                pool.wait_ge(rows_found, 1)
                for t in range(tiles):
                    for u in range(units):
                        for n, group in enumerate(GROUPS):
                            for m in group:
                                at = t * units + u
                                pool.indirect_dma_start(rows[:, at, 4 * n + m, :], None, gathered_tables,
                                                        bass.IndirectOffsetOnAxis(ap=row_at[:, at, 4 * n + m:4 * n + m + 1], axis=0)
                                                        ).then_inc(rows_in[at][n], 16)

            @block.scalar
            def _(act):
                act.dma_start(table_sb[0:hot_rows[0], 0, 0:hot_parts[0] * dim],
                              hot_tables[0].rearrange("(p c) d -> p (c d)", c=hot_parts[0])).then_inc(hot_in[0], 16)
                act.dma_start(dense_rows[:, :, :], dense.rearrange("(t p) d -> p t d", p=P)).then_inc(dense_in, 16)
                act.dma_start(columns_sb[:, :], columns).then_inc(weights_in, 16)

                def place_groups(t, u):
                    if t >= 1:
                        act.wait_ge(gram_done, ((t - 1) * units + u + 1) * halves)
                    for n in act_groups:
                        act.wait_ge(turned[u][n], t + 1)
                        place(act.copy, u, n).then_inc(placed_act, 1)

                def one_hot_part(i):
                    n, c = hot_list[i]
                    r = hot_rows[n]
                    at = act_share.index(i)
                    if at >= 2:
                        act.wait_ge(one_hot_act, at - 1)
                    nc.scalar.activation(distance[0:r, at % 2, :], hot_ids_sb[0:r, n, :], ACT.Abs, scale=-1.0,
                                         bias=row_ids[0:r, n, c:c + 1]).then_inc(distance_made, 1)
                    if i >= ring:
                        act.wait_ge(one_hot_used, i - ring + 1)
                    act.wait_ge(distance_made, at + 1)
                    nc.scalar.activation(one_hot[0:r, i % ring, :], distance[0:r, at % 2, :], ACT.Relu, scale=-1.0,
                                         bias=1.0).then_inc(one_hot_act, 1)

                def high_part(n):
                    act.wait_ge(hot_in[n], 32)
                    if n >= 3:
                        act.wait_ge(one_hot_used, sum(hot_parts[:n - 2]))
                    r = hot_rows[n]
                    for own in split_columns(n):
                        nc.scalar.activation(table_hi[0:r, n % 3, own], table_sb[0:r, n, own], ACT.Copy).then_inc(hi_made, 1)

                def copy_whole(n):
                    act.wait_ge(one_hot_used, sum(hot_parts[:n + 1]))
                    if n == n_hot - 1:
                        act.copy(features_t[:, :, n_hot], hot_bank(n)[:, 0:P]).then_inc(last_placed, 1)
                    nc.scalar.activation(whole_t[:, n + 1, :], hot_bank(n), ACT.Copy).then_inc(whole_made, 1)

                high_part(0)
                act.wait_ge(dense_turned, 1)
                nc.scalar.activation(whole_t[:, 0, :], turn_ps[:, 0, :], ACT.Copy).then_inc(whole_made, 1)
                high_part(1)
                act.wait_ge(row_ids_made, n_hot)
                for n in range(n_hot):
                    share = [i for i in act_share if hot_list[i][0] == n]
                    one_hot_part(share[0])
                    if n >= 1:
                        copy_whole(n - 1)
                    if n + 2 < n_hot:
                        high_part(n + 2)
                    for i in share[1:]:
                        one_hot_part(i)
                    if n - 1 in EARLY:
                        act.wait_ge(start_zeroed, 1)
                        place_groups(0, EARLY.index(n - 1))
                copy_whole(n_hot - 1)
                act.wait_ge(weights_in, 16 * n_weight_loads)

                def plain_pairs(t, u, half):
                    act.wait_ge(gram_done, (t * units + u) * halves + half + 1)
                    for j in range(4):
                        for k in range(4):
                            last = act.copy(*pair_block(t, u, half, j, k, 0, len(range(k, COLUMNS, 4))))
                        last.then_inc(pairs_plain, 1)

                def layer1_relu(t, at):
                    for m in range(n1):
                        if t < tiles - 1:
                            act.wait_ge(layer1_done, (t + 1) * n1)
                        else:
                            act.wait_ge(layer1_done, t * n1 + m + 1)
                        nc.scalar.activation(hidden1_t[:, m, :], at[m], ACT.Relu, bias=b1_sb[:, m:m + 1]).then_inc(layer1_out, 1)

                def layer2_relu(t, at, parts=range(n2)):
                    act.wait_ge(layer2_done, t + 1)
                    for m in parts:
                        nc.scalar.activation(hidden2_t[:, t % 2, m, :], at[m], ACT.Relu, bias=b2_sb[:, m:m + 1]).then_inc(layer2_out, 1)

                def results(t, at):
                    act.wait_ge(layer3_done, t + 1)
                    nc.scalar.activation(y_row[0:1, t * P:(t + 1) * P], at, ACT.Copy).then_inc(y_out, 1)

                for t in range(tiles):
                    plain_pairs(t, 0, 0)
                    if t >= 2:
                        results(t - 2, layer3_at)
                    plain_pairs(t, 0, 1)
                    if t == 0:
                        place_groups(1, 0)
                    if t >= 1:
                        place_groups(t, 1)
                        layer1_relu(t - 1, layer1_at)
                    plain_pairs(t, 1, 0)
                    if 1 <= t < tiles - 1:
                        place_groups(t + 1, 0)
                    plain_pairs(t, 1, 1)
                    if t >= 1:
                        layer2_relu(t - 1, layer2_at)
                layer1_relu(tiles - 1, last_layer1_at)
                layer2_relu(tiles - 1, last_layer2_at, range(n2 - 1))
                results(tiles - 2, layer3_at)
                results(tiles - 1, last_layer3_at)

            @block.vector
            def _(dve):
                nc.vector.memset(features_t[:, :, FEATURES:SLOTS], 0.0).then_inc(start_zeroed, 1)
                nc.vector.memset(pairs[:, :, :, :], 0.0).then_inc(start_zeroed, 1)
                dve.wait_ge(ids_in, 16)
                starts = ids_sb[:, tiles * units:, :].broadcast_to([P, tiles * units, GATHERS])
                nc.vector.tensor_tensor(row_at[:, :, :], ids_sb[:, 0:tiles * units, :], starts, ALU.add).then_inc(rows_found, 1)
                dve.wait_ge(row_ids_made, n_hot)

                def place_whole(t, u):
                    dve.wait_ge(gram_done, ((t - 1) * units + u + 1) * halves)
                    b = t * P + u * unit
                    nc.vector.tensor_copy(slots[:, 0:1 + n_hot, u * unit:(u + 1) * unit],
                                          whole_t[:, :, b:b + unit]).then_inc(whole_placed, 1)

                def place_groups(t, u):
                    if t >= 1:
                        dve.wait_ge(gram_done, ((t - 1) * units + u + 1) * halves)
                    for n in dve_groups:
                        dve.wait_ge(turned[u][n], t + 1)
                        place(nc.vector.tensor_copy, u, n).then_inc(placed_dve, 1)

                def low_part(n):
                    r = hot_rows[n]
                    for piece, own in enumerate(split_columns(n)):
                        dve.wait_ge(hi_made, pieces_made(n) + piece + 1)
                        nc.vector.tensor_tensor(table_lo[0:r, n % 3, own], table_sb[0:r, n, own],
                                                table_hi[0:r, n % 3, own].bitcast(F32), ALU.subtract).then_inc(lo_made, 1)

                low_part(0)
                for i, (n, c) in enumerate(hot_list):
                    r = hot_rows[n]
                    if c == 0:
                        dve.wait_ge(hot_in[n], 32)
                    if i not in act_share:
                        if i >= ring:
                            dve.wait_ge(one_hot_used, i - ring + 1)
                        nc.vector.tensor_scalar(one_hot[0:r, i % ring, :], hot_ids_sb[0:r, n, :], row_ids[0:r, n, c:c + 1],
                                                None, ALU.is_equal).then_inc(one_hot_dve, 1)
                    if c == 1 and n + 1 < n_hot:
                        low_part(n + 1)
                    if c == 4 and n - 1 in EARLY:
                        dve.wait_ge(start_zeroed, 1)
                        place_groups(0, EARLY.index(n - 1))
                dve.wait_ge(weights_in, 16 * n_weight_loads)
                nc.vector.tensor_tensor(w_dense_sum[:, :], w_dense_sb[:, 0, :], w_dense_sb[:, 1, :], ALU.add).then_inc(w_dense_summed, 1)
                dve.wait_ge(whole_made, n_hot)
                nc.vector.tensor_copy(slots[:, 0:n_hot, :], whole_t[:, 0:n_hot, 0:P]).then_inc(whole_placed, 1)
                dve.wait_ge(whole_made, 1 + n_hot)

                def late_pairs(t, u, half):
                    for j in range(4):
                        dve.wait_ge(pairs_plain, ((t * units + u) * halves + half) * 4 + j + 1)
                        for k in range(4):
                            count = len(range(k, FEATURES - COLUMNS, 4))
                            dst, src = pair_block(t, u, half, j, k, COLUMNS, count)
                            late = late_sb[32 * k:32 * k + FEATURES, 0:count].rearrange("p (i o) -> p i o", o=1)
                            last = nc.vector.copy_predicated(dst, late.broadcast_to([FEATURES, count, quads]), src)
                    last.then_inc(pairs_whole, 1)

                for t in range(tiles):
                    if t >= 1:
                        place_whole(t, 1)
                    late_pairs(t, 0, 0)
                    late_pairs(t, 0, 1)
                    if t >= 1:
                        place_groups(t, 1)
                    if t + 1 < tiles:
                        place_whole(t + 1, 0)
                    if t == 0:
                        place_groups(1, 0)
                    late_pairs(t, 1, 0)
                    if 1 <= t < tiles - 1:
                        place_groups(t + 1, 0)
                    late_pairs(t, 1, 1)
                dve.wait_ge(layer2_done, tiles)
                nc.vector.tensor_scalar(hidden2_t[:, (tiles - 1) % 2, n2 - 1, :], last_layer2_at[n2 - 1], b2_sb[:, n2 - 1:n2], 0.0,
                                        ALU.add, ALU.max).then_inc(layer2_out_dve, 1)

            @block.tensor
            def _(pe):
                def transpose_groups(t, u, groups=range(n_groups)):
                    for n in groups:
                        group = GROUPS[n]
                        pe.wait_ge(rows_in[t * units + u][n], 16 * len(group))
                        for m in group:
                            last = nc.tensor.transpose(turn_ps[:, n, m * P:(m + 1) * P], rows[:, t * units + u, 4 * n + m, :], ident[:, :])
                        last.then_inc(turned[u][n], 1)

                def products(t, u, half):
                    if half == 0:
                        if t == 0:
                            pe.wait_ge(whole_placed, 1)
                            pe.wait_ge(last_placed, 1)
                        else:
                            pe.wait_ge(whole_placed, 1 + (t - 1) * units + u + 1)
                        for n in range(n_groups):
                            wait_placed(pe, t, u, n)
                    if t + u > 0:
                        pe.wait_ge(pairs_whole, (t * units + u - 1) * halves + half + 1)
                    else:
                        pe.wait_ge(whole_made, n_hot + half)
                    for q in range(quads):
                        b = u * unit + (half * quads + q) * 4
                        last = nc.tensor.matmul(gram_ps[0:quad_rows, half, q, 0:4 * FEATURES],
                                                flat_features[:, b * SLOTS:b * SLOTS + quad_rows],
                                                features_t[:, b:b + 4, 0:FEATURES], start=True, stop=True)
                    last.then_inc(gram_done, 1)

                def layer1_dense(t, m, at):
                    nc.tensor.matmul(at[m], w_dense_sum[:, m * P:(m + 1) * P], whole_t[:, 0, t * P:(t + 1) * P], start=True, stop=False)

                def layer1_pairs(t, m, at):
                    pe.wait_ge(pairs_whole, (t + 1) * units * halves)
                    for i in range(PAIR_PARTS):
                        last = nc.tensor.matmul(at[m], w_pairs_sb[:, i, m * P:(m + 1) * P], pairs[:, t % 2, i, :],
                                                start=False, stop=(i == PAIR_PARTS - 1))
                    last.then_inc(layer1_done, 1)

                def layer2(t, at):
                    pe.wait_ge(layer1_out, (t + 1) * n1)
                    for m in range(n2):
                        for i in range(n1):
                            last = nc.tensor.matmul(at[m], w2_sb[:, i, m * P:(m + 1) * P],
                                                    hidden1_t[:, i, :], start=(i == 0), stop=(i == n1 - 1))
                    last.then_inc(layer2_done, 1)

                def layer3(t, at, of_act=n2):
                    pe.wait_ge(layer2_out, t * n2 + of_act)
                    for i in range(n2):
                        last = nc.tensor.matmul(at, w3_sb[:, i:i + 1], hidden2_t[:, t % 2, i, :], start=(i == 0), stop=(i == n2 - 1))
                    last.then_inc(layer3_done, 1)

                pe.wait_ge(ident_made, 1)
                pe.wait_ge(dense_in, 16)
                for t in range(tiles):
                    last = nc.tensor.transpose(turn_ps[:, 0, t * P:(t + 1) * P], dense_rows[:, t, :], ident[:, :])
                last.then_inc(dense_turned, 1)
                for i, (n, c) in enumerate(hot_list):
                    r = hot_rows[n]
                    if c == 0 and n >= 2:
                        pe.wait_ge(whole_made, n)
                    if c in (0, hot_parts[0] // 2):
                        pe.wait_ge(lo_made, pieces_made(n) + 1 if c == 0 else pieces_made(n + 1))
                    if i in act_share:
                        pe.wait_ge(one_hot_act, act_share.index(i) + 1)
                    else:
                        pe.wait_ge(one_hot_dve, i + 1 - len([a for a in act_share if a < i]))
                    nc.tensor.matmul(hot_bank(n), table_hi[0:r, n % 3, c * dim:(c + 1) * dim],
                                     one_hot[0:r, i % ring, :], start=(c == 0), stop=False)
                    nc.tensor.matmul(hot_bank(n), table_lo[0:r, n % 3, c * dim:(c + 1) * dim],
                                     one_hot[0:r, i % ring, :], start=False, stop=(c == hot_parts[n] - 1)).then_inc(one_hot_used, 1)
                    if c == hot_parts[n] - 1 and n in EARLY:
                        u = EARLY.index(n)
                        pe.wait_ge(whole_made, 1)
                        if u == 1:
                            for g in range(n_groups):
                                wait_placed(pe, 0, 0, g)
                        transpose_groups(0, u)
                pe.wait_ge(w_dense_summed, 1)

                rows_before = [None, (2,2,2), (2,2,2), (3,3,4)]
                soon = range(n_groups)
                for t in range(tiles):
                    products(t, 0, 0)
                    if t >= 2:
                        layer3(t - 2, layer3_at)
                    products(t, 0, 1)
                    if t >= 1:
                        if t >= 2:
                            pe.wait_ge(y_out, t - 1)
                        for m in range(n1):
                            for g in range(n_groups):
                                if m == rows_before[t][g]:
                                    transpose_groups(t, 1, [g])
                            layer1_dense(t - 1, m, layer1_at)
                            layer1_pairs(t - 1, m, layer1_at)
                        for g in range(n_groups):
                            if rows_before[t][g] == n1:
                                transpose_groups(t, 1, [g])
                    else:
                        transpose_groups(1, 0)
                    products(t, 1, 0)
                    products(t, 1, 1)
                    if 1 <= t < tiles - 1:
                        transpose_groups(t + 1, 0, soon if t == 1 else soon[:-1])
                    if t >= 1:
                        layer2(t - 1, layer2_at)
                    if 1 <= t < tiles - 1:
                        transpose_groups(t + 1, 0, () if t == 1 else soon[-1:])
                pe.wait_ge(pairs_whole, tiles * units * halves - 1)
                for m in range(n1):
                    layer1_dense(tiles - 1, m, last_layer1_at)
                for m in range(n1):
                    layer1_pairs(tiles - 1, m, last_layer1_at)
                for i in range(n1):
                    pe.wait_ge(layer1_out, (tiles - 1) * n1 + i + 1)
                    for m in range(n2):
                        last = nc.tensor.matmul(last_layer2_at[m], w2_sb[:, i, m * P:(m + 1) * P],
                                                hidden1_t[:, i, :], start=(i == 0), stop=(i == n1 - 1))
                last.then_inc(layer2_done, 1)
                layer3(tiles - 2, layer3_at)
                pe.wait_ge(layer2_out_dve, 1)
                layer3(tiles - 1, last_layer3_at, of_act=n2 - 1)


def kernel(**inputs):
    import numpy as _np
    import concourse.bacc as _bacc
    from concourse import mybir as _mybir
    from concourse.bass_utils import run_bass_kernel_spmd as _run

    nc = _bacc.Bacc("TRN2", target_bir_lowering=False, num_devices=1)
    arrays = {}

    def give(name, a):
        a = _np.ascontiguousarray(a)
        arrays[f"in_{name}"] = a
        return nc.dram_tensor(f"in_{name}", a.shape, _mybir.dt.from_np(a.dtype), kind="ExternalInput").ap()

    w1 = _np.asarray(inputs["W_top1"])
    dim = inputs["r_dense_features"].shape[1]
    pair_row = {}
    for a in range(FEATURES):
        for b in range(a + 1, FEATURES):
            pair_row[a, b] = dim + len(pair_row)
    w_pairs = _np.zeros((128, PAIR_PARTS, w1.shape[1]), w1.dtype)
    late_rows = _np.zeros((128, PAIR_PARTS), _np.int32)
    for p, i, pair, late in pair_places():
        if pair is not None:
            w_pairs[p, i] = w1[pair_row[tuple(sorted(FEATURE_OF[s] for s in pair))]]
            late_rows[p, i] = late
    w_dense = _np.stack([w1[:dim], w1[dim + len(pair_row):]])
    columns = _np.concatenate([_np.asarray(inputs[n]).reshape(-1, 128).T for n in ("b_top1", "b_top2", "W_top3")], axis=1)

    tables = [_np.asarray(inputs[f"tbl_{i}"]) for i in range(TABLES)]
    ids = _np.asarray(inputs["ids"])
    gather_ids = ids[:, list(GATHERED)].reshape(-1, 64, GATHERS, 2).transpose(3, 1, 0, 2).reshape(128, -1, GATHERS)
    starts = _np.cumsum([0] + [tables[i].shape[0] for i in GATHERED])[:-1].astype(_np.int32)
    table_starts = _np.repeat(starts.reshape(GATHERS, 2).T, 64, axis=0)

    args = [
        give("ids", _np.concatenate([gather_ids, table_starts[:, None]], axis=1)),
        give("gathered_tables", _np.concatenate([tables[i] for i in GATHERED])),
        give("hot_ids", ids.T[list(HOT)]),
        [give(f"tbl_{i}", tables[i]) for i in HOT],
        give("dense", inputs["r_dense_features"]),
        give("w_dense", w_dense),
        give("w_pairs", w_pairs),
        give("w2", inputs["W_top2"]),
        give("columns", columns),
        give("late_rows", late_rows),
    ]
    y = nc.dram_tensor("y", (inputs["ids"].shape[0], 1), _mybir.dt.float32, kind="ExternalOutput").ap()
    dlrm_program(nc, *args, y)
    r = _run(nc, [arrays], core_ids=[0])
    return r.results[0]["y"]
```
